# Optimizing a Trainium2 kernel written in Bass

```python
import numpy as np
import jax
import jax.numpy as jnp

def _softmax(x, axis=-1):
    return jax.nn.softmax(x, axis=axis)

def _gelu(x):
    return jax.nn.gelu(x, approximate=True)

def _silu(x):
    return jax.nn.silu(x)

def _sigmoid(x):
    return jax.nn.sigmoid(x)

def _layernorm(x, axis=-1, eps=1e-05):
    m = jnp.mean(x, axis=axis, keepdims=True)
    v = jnp.var(x, axis=axis, keepdims=True)
    return (x - m) / jnp.sqrt(v + eps)

def _scatter_add(tgt, idx, src, axis=0):
    return tgt.at[idx].add(src)

def _segment_sum(src, seg, n):
    return jax.ops.segment_sum(src, seg, n)
kernel_name = 'mk_macaron_d1_jaxref_r8_d4d0e9'

def setup_inputs(seed: int=0):
    np.random.seed(seed)
    _w = jnp.asarray

    def _L0_attn_setup():
        import jax, jax.numpy as jnp
        import numpy as np
        EPS = 1e-05
        key = jax.random.key(seed)
        ks = jax.random.split(key, 16)
        B, T, D = (8, 256, 128)
        Hh, KD, VD, LR, GLR = (4, 64, 128, 32, 64)
        s = 0.02
        w = lambda k, shape: jax.random.normal(k, shape, jnp.float32) * s
        return {'hidden_states': jax.random.normal(ks[0], (B, T, D), jnp.float32), 'mu_x': w(ks[1], (D,)), 'W_x1': w(ks[2], (5 * LR, D)), 'W_x2': w(ks[3], (D, 5 * LR)), 'x_bias': jnp.zeros((5, D), jnp.float32), 'W_r': w(ks[4], (KD, D)), 'W_k': w(ks[5], (KD, D)), 'W_v': w(ks[6], (VD, D)), 'W_g': w(ks[7], (VD, D)), 'A_w': w(ks[8], (GLR, D)), 'B_w': w(ks[9], (KD, GLR)), 'b_w': jnp.zeros((KD,), jnp.float32), 'bonus': w(ks[10], (Hh, KD // Hh)), 'gn_weight': jnp.ones((VD,), jnp.float32), 'gn_bias': jnp.zeros((VD,), jnp.float32), 'W_o': w(ks[11], (D, VD))}
    _L0_attn_in = _L0_attn_setup()

    def _L0_ffn_setup():
        import jax, jax.numpy as jnp
        import numpy as np
        B, N, C, F, E, K = (2, 256, 128, 512, 8, 2)
        key = jax.random.key(seed)
        k = jax.random.split(key, 6)
        xavier1 = float(np.sqrt(6.0 / (C + F)))
        xavier2 = float(np.sqrt(6.0 / (F + C)))
        return {'x': jax.random.normal(k[0], (B, N, C), dtype=jnp.float32), 'router_w': jax.random.normal(k[1], (E, C), dtype=jnp.float32) * 0.01, 'w1': jax.random.uniform(k[2], (E, F, C), dtype=jnp.float32, minval=-xavier1, maxval=xavier1), 'b1': jnp.zeros((E, F), dtype=jnp.float32), 'w2': jax.random.uniform(k[3], (E, C, F), dtype=jnp.float32, minval=-xavier2, maxval=xavier2), 'b2': jnp.zeros((E, C), dtype=jnp.float32)}
    _L0_ffn_in = _L0_ffn_setup()
    _d = {'L0_attn_hidden_states': _L0_attn_in['hidden_states'], 'L0_attn_mu_x': _L0_attn_in['mu_x'], 'L0_attn_W_x1': _L0_attn_in['W_x1'], 'L0_attn_W_x2': _L0_attn_in['W_x2'], 'L0_attn_x_bias': _L0_attn_in['x_bias'], 'L0_attn_W_r': _L0_attn_in['W_r'], 'L0_attn_W_k': _L0_attn_in['W_k'], 'L0_attn_W_v': _L0_attn_in['W_v'], 'L0_attn_W_g': _L0_attn_in['W_g'], 'L0_attn_A_w': _L0_attn_in['A_w'], 'L0_attn_B_w': _L0_attn_in['B_w'], 'L0_attn_b_w': _L0_attn_in['b_w'], 'L0_attn_bonus': _L0_attn_in['bonus'], 'L0_attn_gn_weight': _L0_attn_in['gn_weight'], 'L0_attn_gn_bias': _L0_attn_in['gn_bias'], 'L0_attn_W_o': _L0_attn_in['W_o'], 'L0_ffn_router_w': _L0_ffn_in['router_w'], 'L0_ffn_w1': _L0_ffn_in['w1'], 'L0_ffn_b1': _L0_ffn_in['b1'], 'L0_ffn_w2': _L0_ffn_in['w2'], 'L0_ffn_b2': _L0_ffn_in['b2']}
    _x0 = _d['L0_attn_hidden_states']
    _d['L0_attn_hidden_states'] = jax.random.normal(jax.random.fold_in(jax.random.key(seed), 1), (2, 1024, 128), dtype=_x0.dtype)
    del _x0
    return _d

def reference(L0_attn_hidden_states, L0_attn_mu_x, L0_attn_W_x1, L0_attn_W_x2, L0_attn_x_bias, L0_attn_W_r, L0_attn_W_k, L0_attn_W_v, L0_attn_W_g, L0_attn_A_w, L0_attn_B_w, L0_attn_b_w, L0_attn_bonus, L0_attn_gn_weight, L0_attn_gn_bias, L0_attn_W_o, L0_ffn_router_w, L0_ffn_w1, L0_ffn_b1, L0_ffn_w2, L0_ffn_b2):

    def _L0_attn_ref(hidden_states, mu_x, W_x1, W_x2, x_bias, W_r, W_k, W_v, W_g, A_w, B_w, b_w, bonus, gn_weight, gn_bias, W_o):
        import jax, jax.numpy as jnp
        import numpy as np
        EPS = 1e-05
        B, T, D = hidden_states.shape
        Hh = bonus.shape[0]
        x = hidden_states
        shifted = jnp.pad(x, ((0, 0), (1, 0), (0, 0)))[:, :T]
        delta = shifted - x
        lr = W_x1.shape[0] // 5
        z = jnp.tanh((x + delta * mu_x) @ W_x1.T).reshape(B, T, 5, lr)
        mus = jnp.einsum('blnr,dnr->blnd', z, W_x2.reshape(D, 5, lr)) + x_bias
        r_mu, w_mu, k_mu, v_mu, g_mu = (mus[:, :, i] for i in range(5))
        r = (x + delta * r_mu) @ W_r.T
        w = jnp.tanh((x + delta * w_mu) @ A_w.T) @ B_w.T + b_w
        k = (x + delta * k_mu) @ W_k.T
        v = (x + delta * v_mu) @ W_v.T
        g = (x + delta * g_mu) @ W_g.T
        K = W_r.shape[0] // Hh
        V = W_v.shape[0] // Hh
        r = r.reshape(B, T, Hh, K)
        k = k.reshape(B, T, Hh, K)
        w = -jnp.exp(w.reshape(B, T, Hh, K))
        v = v.reshape(B, T, Hh, V)
        u = bonus

        def step(S, inp):
            q_t, k_t, v_t, w_t = inp
            kv = k_t[..., :, None] * v_t[..., None, :]
            o_t = jnp.einsum('bhk,bhkv->bhv', q_t, S + u[None, :, :, None] * kv)
            S = jnp.exp(w_t)[..., None] * S + kv
            return (S, o_t)
        S0 = jnp.zeros((B, Hh, K, V), dtype=x.dtype)
        xs = (jnp.swapaxes(r, 0, 1), jnp.swapaxes(k, 0, 1), jnp.swapaxes(v, 0, 1), jnp.swapaxes(w, 0, 1))
        _, o = jax.lax.scan(step, S0, xs)
        o = jnp.swapaxes(o, 0, 1)
        mean = o.mean(-1, keepdims=True)
        var = o.var(-1, keepdims=True)
        o = (o - mean) / jnp.sqrt(var + EPS)
        o = o.reshape(B, T, Hh * V) * gn_weight + gn_bias
        o = o * jax.nn.silu(g)
        return o @ W_o.T

    def _L0_ffn_ref(x, router_w, w1, b1, w2, b2):
        import jax, jax.numpy as jnp
        import numpy as np
        B, N, C, F, E, K = (2, 256, 128, 512, 8, 2)
        Bb, Nn, Cc = x.shape
        x_flat = x.reshape(-1, Cc)
        logits = jnp.einsum('tc,ec->te', x_flat, router_w)
        probs = jax.nn.softmax(logits, axis=-1)
        top_w, top_idx = jax.lax.top_k(probs, K)
        top_w = top_w / (jnp.sum(top_w, axis=-1, keepdims=True) + 1e-09)
        h = jnp.einsum('tc,efc->tef', x_flat, w1) + b1[None]
        h = jax.nn.relu(h)
        y = jnp.einsum('tef,ecf->tec', h, w2) + b2[None]
        sel = jnp.take_along_axis(y, top_idx[:, :, None], axis=1)
        out = jnp.einsum('tkc,tk->tc', sel, top_w)
        return out.reshape(Bb, Nn, Cc)
    x = L0_attn_hidden_states
    x = x + 0.5 * _L0_ffn_ref(_layernorm(x, axis=-1), L0_ffn_router_w, L0_ffn_w1, L0_ffn_b1, L0_ffn_w2, L0_ffn_b2)
    x = x + _L0_attn_ref(_layernorm(x, axis=-1), L0_attn_mu_x, L0_attn_W_x1, L0_attn_W_x2, L0_attn_x_bias, L0_attn_W_r, L0_attn_W_k, L0_attn_W_v, L0_attn_W_g, L0_attn_A_w, L0_attn_B_w, L0_attn_b_w, L0_attn_bonus, L0_attn_gn_weight, L0_attn_gn_bias, L0_attn_W_o)
    x = x + 0.5 * _L0_ffn_ref(_layernorm(x, axis=-1), L0_ffn_router_w, L0_ffn_w1, L0_ffn_b1, L0_ffn_w2, L0_ffn_b2)
    return x

_drawn_inputs = setup_inputs


def setup_inputs(seed=0):
    import zlib

    import numpy as np

    out = dict(_drawn_inputs(seed))
    spreads = {'L0_attn_x_bias': (0.0, 0.379),
     'L0_attn_b_w': (0.0, 0.8),
     'L0_attn_gn_weight': (1.0, 0.6),
     'L0_attn_gn_bias': (0.0, 0.8),
     'L0_ffn_b1': (0.0, 0.1),
     'L0_ffn_b2': (0.0, 0.1)}
    factors = {'L0_attn_mu_x': 8.0,
     'L0_attn_W_x1': 8.0,
     'L0_attn_W_x2': 8.0,
     'L0_attn_A_w': 8.0,
     'L0_attn_B_w': 8.0,
     'L0_attn_bonus': 8.0}
    for name, (base, spread) in spreads.items():
        noise = np.random.default_rng([zlib.crc32(name.encode()), seed]).standard_normal(out[name].shape)
        drawn = base * np.exp(spread * noise) if base else spread * noise
        out[name] = jnp.asarray(drawn.astype(out[name].dtype))
    for name, factor in factors.items():
        out[name] = (out[name] * factor).astype(out[name].dtype)
    return out
```

```python
from contextlib import ExitStack

import concourse.bass as bass
from concourse import mybir

ALU = mybir.AluOpType
ACT = mybir.ActivationFunctionType
AX = mybir.AxisListType
F32 = mybir.dt.float32
F32R = mybir.dt.float32r

P = 128
NB = 2
NT = 512
E, FC = 8, 4
STEPS = NB * E
KD, NH, NV = 16, 4, 32
NG, VG = 2, 16
BH = NB * NH
EPS = 1e-5
STAGES = [(0, None), (1, 0), (0, 1), (1, None)]
LN_OF_FFN = [0, 2, 4, 5]
LN_OF_ATT = {0: 1, 1: 3}
H32, HS, TS, QS, SS = 4, 6, 4, 8, 4

C_ID, C_RED, C_CEN, C_AVG, C_BET, C_TIE = 0, 128, 256, 512, 640, 768
C_SEL = C_TIE + 64
C_ALL = C_SEL + VG * P
W_X1, W_X2, W_X2B, W_R, W_K, W_A, W_B = 0, 160, 288, 416, 480, 544, 608
W_V = 672
W_G = W_V + NG * NB * P
W_O = W_G + NG * NB * P
W_RT = W_O + NG * NB * P
W_B1, W_B2 = W_RT + E, W_RT + E + E * FC
W_MU, W_XB = W_B2 + E, W_B2 + E + 1
W_BW, W_U, W_GW, W_GB = W_XB + 5, W_XB + 6, W_XB + 7, W_XB + 7 + NG
W_ALL = W_GB + NG


def program(nc, xT_in, wexp_in, small_in, const_in, out):
    with ExitStack() as ctx:
        def sb(name, shape, dt=F32):
            return ctx.enter_context(nc.sbuf_tensor(name, shape, dt))

        def sem(name):
            return ctx.enter_context(nc.semaphore(name))

        xT = sb("xT", [P, 2, NB, NT])
        pool_a = sb("pool_a", [P, 10 * NT])
        wraw = pool_a[:, 0:4 * NT].rearrange("p (a n) -> p a n", a=2)
        sel_raw = pool_a[:, 4 * NT:8 * NT]
        u = pool_a[:, :].rearrange("p (i b n) -> p i b n", i=5, b=NB)
        kv = pool_a[:, 0:2 * NT].rearrange("p (a n) -> p a n", a=2)
        o = pool_a[:, 2 * NT:4 * NT].rearrange("p (g n) -> p g n", g=NG)
        S = pool_a[:, 4 * NT:4 * NT + SS * (NT + 1)].rearrange("p (a n) -> p a n", a=SS)
        whi = sb("whi", [P, E, 2, FC, P], F32R)
        wlo = sb("wlo", [P, E, 2, FC, P], F32R)
        small = sb("small", [P, W_ALL])
        const = sb("const", [P, C_SEL])
        sel = sb("sel", [P, VG, P], F32R)
        rwh = sb("rwh", [P, 2, E], F32R)
        mv = sb("mv", [P, 8, 2])
        bst = sb("bst", [P, 8, 6])
        std = sb("std", [P, 8])
        rstd = sb("rstd", [P, 8])
        epsc = sb("epsc", [P, 1])
        xnt = sb("xnt", [P, 8, P])
        aw = xnt[:, 0:4, :].rearrange("p a n -> p (a n)")
        quk = xnt[:, 4:8, :].rearrange("p a n -> p (a n)")
        xhi = sb("xhi", [P, NB, NT], F32R)
        xlo = sb("xlo", [P, NB, NT], F32R)
        rt = sb("rt", [P, 8, 8, E])
        rs = sb("rs", [P, 8, 8])
        gate = sb("gate", [P, 8, E])
        G = sb("G", [P, 2, NT])
        h32 = sb("h32", [P, H32, NT])
        hhi = sb("hhi", [P, HS, NT], F32R)
        hlo = sb("hlo", [P, HS, NT], F32R)
        gy = sb("gy", [P, 2, NT])
        xa = sb("xa", [P, NB, NT + 1])
        qs = sb("qs", [P, QS, NT])
        delta, xm, z0, z1 = qs[:, 0:2, :], qs[:, 2:4, :], qs[:, 4:6, :], qs[0:32, 6:8, :]
        mix = h32
        q = sb("q", [P, NT])
        kk = sb("kk", [P, NT])
        dec = sb("dec", [P, NT])
        vhi = sb("vhi", [P, NG, NT], F32R)
        vlo = sb("vlo", [P, NG, NT], F32R)
        sg = sb("sg", [P, NG, NT])
        carry = sb("carry", [P, NV])

        U = [ctx.enter_context(nc.psum_tensor(f"U{i}", [P, NT], F32)) for i in range(3)]
        Y = [ctx.enter_context(nc.psum_tensor(f"Y{i}", [P, NT], F32)) for i in range(2)]
        R = [ctx.enter_context(nc.psum_tensor(f"R{i}", [P, NT], F32)) for i in range(2)]
        OB = ctx.enter_context(nc.psum_tensor("OB", [P, NT], F32))
        MIXB = U + Y + R + [OB]

        ident = const[:, C_ID:C_ID + P]
        tie = const[:, C_TIE:C_TIE + 64].rearrange("p (t e) -> p t e", e=E)

        def w(at, n, rows=slice(0, P)):
            return small[rows, at:at + n]

        x_in, w_in, small_l, const_l, sel_l, out_done = sem("x_in"), [sem("w_in0"), sem("w_in1")], sem("small_in"), sem("const_in"), sem("sel_in"), sem("out_done")
        whi_s, wlo_s, setup = sem("w_hi"), sem("w_lo"), sem("setup")
        ln_src, ln_var, ln_std, ln_nrm, ln_T = (sem(n) for n in ("ln_src", "ln_var", "ln_std", "ln_nrm", "ln_T"))
        xn_hi, xn_lo, xa_rdy = sem("xn_hi"), sem("xn_lo"), sem("xa_rdy")
        lg, lg_sub, p_exp, gates = sem("logits"), sem("logits_sub"), sem("p_exp"), sem("gates")
        up, h_f, h_hi, h_lo = sem("up"), sem("h_f"), sem("h_hi"), sem("h_lo")
        g_T, g_c, down, comb, acc = sem("g_T"), sem("g_c"), sem("down"), sem("comb"), sem("acc")
        dch, pch, ach = sem("dve_chain"), sem("pool_chain"), sem("act_chain")
        xm_r, z_p, z_r, mus, mterm, u_r = sem("xm_r"), sem("z_p"), sem("z_r"), sem("mus"), sem("mterm"), sem("u_r")
        pr, aw_r, wb_r, att_in = sem("proj"), sem("aw_r"), sem("wb_r"), sem("att_in")
        sg_r, quk_r, bet, bv_r, vlo_r, bet_c, sel_r = sem("sg_r"), sem("quk_r"), sem("beta"), sem("bv_r"), sem("vlo_r"), sem("beta_c"), sem("sel_r")
        vb, kv_r, st_r, qs_r, red, o_r = sem("vb"), sem("kv_r"), sem("st_r"), sem("qs_r"), sem("red"), sem("o_r")
        seed, xa_prev, s_zero = sem("seed"), sem("xa_prev"), sem("s_zero")
        cen, sq_r, var_p, sd_r, yo_r, yp, x_att = sem("cen"), sem("sq_r"), sem("var_p"), sem("sd_r"), sem("yo_r"), sem("yp"), sem("x_att")

        block = ctx.enter_context(nc.Block())

        @block.sync
        def _(sp):
            xi = xT_in.rearrange("p (h b n) -> p h b n", h=2, b=NB)
            sp.dma_start(xT[:, 0, :, :], xi[:, 0]).then_inc(x_in, 16)
            sp.dma_start(const[:, :], const_in[:, 0:C_SEL]).then_inc(const_l, 16)
            for e in range(E):
                if e >= 2:
                    sp.wait_ge(whi_s, e - 1)
                    sp.wait_ge(wlo_s, e - 1)
                sp.dma_start(wraw[:, e % 2, :], wexp_in[:, e * 2 * NT:(e + 1) * 2 * NT]).then_inc(w_in[e % 2], 16)
                if e == 1:
                    sp.dma_start(small[:, :], small_in).then_inc(small_l, 16)
            sp.dma_start(sel_raw, const_in[:, C_SEL:C_ALL]).then_inc(sel_l, 16)
            sp.dma_start(xT[:, 1, :, :], xi[:, 1]).then_inc(x_in, 16)
            ov = out.rearrange("p (h b n) -> p h b n", h=2, b=NB)
            for s in (2, 3):
                for b in range(NB):
                    sp.wait_ge(acc, s * STEPS + (b + 1) * E)
                    sp.dma_start(ov[:, s - 2, b], xT[:, s - 2, b, :]).then_inc(out_done, 16)
            sp.wait_ge(out_done, 64)

        @block.tensor
        def _(pe):
            mm = pe.matmul

            def norm(L, half):
                for b in range(NB):
                    for t in range(4):
                        last = pe.transpose(U[b][:, t * P:(t + 1) * P], xT[:, half, b, t * P:(t + 1) * P], ident)
                last.then_inc(ln_src, 1)
                pe.wait_ge(ln_nrm, L + 1)
                for b in range(NB):
                    for t in range(4):
                        last = pe.transpose(R[b][:, t * P:(t + 1) * P], xnt[:, 4 * b + t, :], ident)
                last.then_inc(ln_T, 1)

            def router(s):
                pe.wait_ge(xn_hi, 2 * s + 2)
                pe.wait_ge(xn_lo, 2 * s + 2)
                for b in range(NB):
                    for t in range(4):
                        dst = OB[:, (4 * b + t) * E:(4 * b + t + 1) * E]
                        for n, (x, r) in enumerate(((xlo, 1), (xlo, 0), (xhi, 1), (xhi, 0))):
                            last = mm(dst, x[:, b, t * P:(t + 1) * P], rwh[:, r, :], start=(n == 0), stop=(n == 3))
                last.then_inc(lg, 1)

            def ffn_up(s, i, f):
                b, e = divmod(i, E)
                n = (s * STEPS + i) * FC + f
                if n >= 3:
                    pe.wait_ge(h_f, n - 2)
                dst = U[n % 3][:, :]
                mm(dst, wlo[:, e, 0, f, :], xhi[:, b, :], start=True, stop=False)
                mm(dst, whi[:, e, 0, f, :], xlo[:, b, :], start=False, stop=False)
                mm(dst, whi[:, e, 0, f, :], xhi[:, b, :], start=False, stop=True).then_inc(up, 1)

            def ffn_down(s, i, f):
                b, e = divmod(i, E)
                g = s * STEPS + i
                n = g * FC + f
                if f == 0 and g >= 2:
                    pe.wait_ge(comb, g - 1)
                pe.wait_ge(h_lo, n + 1)
                dst = Y[g % 2][:, :]
                mm(dst, wlo[:, e, 1, f, :], hhi[:, n % HS, :], start=(f == 0), stop=False)
                mm(dst, whi[:, e, 1, f, :], hlo[:, n % HS, :], start=False, stop=False)
                last = mm(dst, whi[:, e, 1, f, :], hhi[:, n % HS, :], start=False, stop=(f == FC - 1))
                last.then_inc(down, 1)

            def gates_out(s, i, bank):
                b, e = divmod(i, E)
                for t in range(4):
                    col = gate[:, 4 * b + t, e:e + 1].to_broadcast([P, P])
                    last = pe.transpose(R[bank][:, t * P:(t + 1) * P], col, ident)
                last.then_inc(g_T, 1)

            def v_spread(h, m, bank):
                g, j = order(m)
                mm(R[bank][:, :], sel[:, j, :], vlo[:, g, :], start=True, stop=False)
                mm(R[bank][:, :], sel[:, j, :], vhi[:, g, :], start=False, stop=True).then_inc(vb, 1)

            def reduce(h, n):
                pe.wait_ge(qs_r, h * NV + 4 * n + 4)
                if n % 4 == 0:
                    pe.wait_ge(o_r, h * NG + n // 4)
                c0 = C_RED + 32 * (n % 4)
                for c in range(4):
                    last = mm(OB[32 * c:32 * c + 32, :], const[:, c0:c0 + 32], qs[:, (4 * n + c) % QS, :],
                              start=(n % 4 == 0), stop=(n % 4 == 3))
                last.then_inc(red, 1)

            def attention_in(h):
                L = LN_OF_ATT[h]
                norm(L, h)
                pe.wait_ge(xm_r, h + 1)
                pe.wait_ge(xa_rdy, 2 * h + 2)
                for b in range(NB):
                    mm(U[b][:, :], w(W_X1, P), xm[:, b, :], start=True, stop=True)
                    mm(Y[b][0:32, :], w(W_X1 + P, 32), xm[:, b, :], start=True, stop=True).then_inc(z_p, 1)
                pe.wait_ge(z_r, 4 * h + 4)
                for n in range(5 * NB):
                    i, b = divmod(n, NB)
                    if n >= 8:
                        pe.wait_ge(mterm, 10 * h + n - 7)
                    lhsT = w(W_X2, P, slice(32 * i, 32 * i + 32)) if i < 4 else w(W_X2B, P, slice(0, 32))
                    rhs = z0[32 * i:32 * i + 32, b, :] if i < 4 else z1[:, b, :]
                    mm(MIXB[n % 8][:, :], lhsT, rhs, start=True, stop=True).then_inc(mus, 1)
                pe.wait_ge(mterm, 10 * h + 10)
                pe.wait_ge(u_r, 10 * h + 10)
                for b in range(NB):
                    hb = slice(64 * b, 64 * b + 64)
                    mm(U[2][hb, :], w(W_A, 64), u[:, 1, b, :], start=True, stop=True)
                    mm(U[0][hb, :], w(W_R, 64), u[:, 0, b, :], start=True, stop=True)
                    last = mm(U[1][hb, :], w(W_K, 64), u[:, 2, b, :], start=True, stop=True)
                last.then_inc(pr, 1)
                for g in range(NG):
                    for b in range(NB):
                        last = mm(Y[g][:, :], w(W_V + (g * NB + b) * P, P), u[:, 3, b, :], start=(b == 0), stop=(b == 1))
                    last.then_inc(pr, 1)
                for g in range(NG):
                    for b in range(NB):
                        last = mm(R[g][:, :], w(W_G + (g * NB + b) * P, P), u[:, 4, b, :], start=(b == 0), stop=(b == 1))
                    last.then_inc(pr, 1)
                pe.wait_ge(aw_r, h + 1)
                for b in range(NB):
                    hb = slice(64 * b, 64 * b + 64)
                    last = mm(OB[hb, :], w(W_B, 64, hb), aw[hb, :], start=True, stop=True)
                last.then_inc(wb_r, 1)
                pe.wait_ge(quk_r, h + 1)
                mm(U[2][:, :], const[:, C_BET:C_BET + P], quk[:, :], start=True, stop=True).then_inc(bet, 1)

            def attention_out(h):
                pe.wait_ge(o_r, NG * (h + 1))
                for g in range(NG):
                    for g2 in range(NG):
                        c0 = C_CEN if g == g2 else C_CEN + P
                        last = mm(U[g][:, :], const[:, c0:c0 + P], o[:, g2, :], start=(g2 == 0), stop=(g2 == 1))
                    last.then_inc(cen, 1)
                pe.wait_ge(sq_r, NG * (h + 1))
                for g in range(NG):
                    last = mm(U[2][:, :], const[:, C_AVG:C_AVG + P], xm[:, g, :], start=(g == 0), stop=(g == 1))
                last.then_inc(var_p, 1)
                pe.wait_ge(yo_r, NG * (h + 1))
                pe.wait_ge(comb, (h + 2) * STEPS)
                for b in range(NB):
                    for g in range(NG):
                        last = mm(Y[b][:, :], w(W_O + (g * NB + b) * P, P), o[:, g, :], start=(g == 0), stop=(g == 1))
                    last.then_inc(yp, 1)

            pe.wait_ge(const_l, 16)
            pe.wait_ge(x_in, 16)
            for s, (half, h) in enumerate(STAGES):
                if s == 1:
                    pe.wait_ge(x_in, 32)
                if h is not None:
                    if h == 0:
                        pe.wait_ge(small_l, 16)
                    pe.wait_ge(acc, s * STEPS)
                    pe.wait_ge(g_c, s * STEPS)
                    attention_in(h)
                    pe.wait_ge(bv_r, NG * (h + 1))
                    pe.wait_ge(att_in, h + 1)
                    pe.wait_ge(sel_r, 1)
                    pe.wait_ge(vlo_r, NG * (h + 1))
                    pe.wait_ge(sg_r, NG * (h + 1))
                if s >= 2:
                    pe.wait_ge(x_att, NB * (s - 1))
                    pe.wait_ge(g_c, s * STEPS)
                norm(LN_OF_FFN[s], half)
                router(s)
                nr = 0
                for i in range(STEPS + 1):
                    for f in range(FC):
                        if i < STEPS:
                            if s == 0:
                                pe.wait_ge(wlo_s, i % E + 1)
                                pe.wait_ge(whi_s, i % E + 1)
                            ffn_up(s, i, f)
                        if i > 0:
                            ffn_down(s, i - 1, f)
                    if i < STEPS:
                        g = s * STEPS + i
                        pe.wait_ge(gates, s + 1)
                        if h is None:
                            if i >= 2:
                                pe.wait_ge(g_c, g - 1)
                            gates_out(s, i, i % 2)
                        else:
                            if i >= 1:
                                pe.wait_ge(kv_r, h * NV + 2 * i - 1)
                            gates_out(s, i, i % 2)
                            if i >= 1:
                                pe.wait_ge(kv_r, h * NV + 2 * i)
                            v_spread(h, 2 * i, (i + 1) % 2)
                            pe.wait_ge(g_c, g + 1)
                            v_spread(h, 2 * i + 1, i % 2)
                            if i >= 3 and i % 2 == 1:
                                reduce(h, (i - 3) // 2)
                if h is not None:
                    reduce(h, 7)
                    attention_out(h)

        @block.scalar
        def _(act):
            def split_w(e):
                act.wait_ge(w_in[e % 2], 16 * (e // 2 + 1))
                act.activation(whi[:, e].rearrange("p a f n -> p (a f n)"), wraw[:, e % 2, :], ACT.Copy).then_inc(whi_s, 1)

            def norm_std(L):
                act.wait_ge(ln_var, L + 1)
                act.activation(std[:, :], mv[:, :, 1], ACT.Sqrt, bias=epsc[:, 0:1]).then_inc(ln_std, 1)
                act.wait_ge(ln_T, L + 1)

            def attention_in(h):
                norm_std(LN_OF_ATT[h])
                for b in range(NB):
                    act.activation(xa[:, b, 1:NT + 1], R[b][:, :], ACT.Copy).then_inc(xa_rdy, 1)
                for b in range(NB):
                    act.wait_ge(z_p, NB * h + b + 1)
                    act.activation(z0[:, b, :], U[b][:, :], ACT.Tanh).then_inc(z_r, 1)
                    act.activation(z1[:, b, :], Y[b][0:32, :], ACT.Tanh).then_inc(z_r, 1)
                act.wait_ge(pr, 5 * h + 1)
                act.activation(aw[:, :], U[2][:, :], ACT.Tanh).then_inc(aw_r, 1)
                act.activation(q[:, :], U[0][:, :], ACT.Copy).then_inc(ach, 1)
                act.activation(kk[:, :], U[1][:, :], ACT.Copy).then_inc(ach, 1)
                for g in range(NG):
                    act.wait_ge(pr, 5 * h + 2 + g)
                    act.activation(vhi[:, g, :], Y[g][:, :], ACT.Copy).then_inc(ach, 1)
                for g in range(NG):
                    act.wait_ge(pr, 5 * h + 4 + g)
                    act.activation(sg[:, g, :], R[g][:, :], ACT.Tanh, scale=0.5).then_inc(ach, 1)
                act.wait_ge(wb_r, h + 1)
                act.activation(dec[:, :], OB[:, :], ACT.Exp, bias=w(W_BW, 1)).then_inc(ach, 1)
                act.wait_ge(ach, 7 * (h + 1))
                act.activation(dec[:, :], dec[:, :], ACT.Exp, scale=-1.0).then_inc(att_in, 1)
                act.wait_ge(bet, h + 1)
                act.activation(aw[:, :], U[2][:, :], ACT.Copy).then_inc(bet_c, 1)

            def attention_out(h):
                for g in range(NG):
                    act.wait_ge(cen, NG * h + g + 1)
                    act.activation(xm[:, g, :], U[g][:, :], ACT.Square).then_inc(sq_r, 1)
                act.wait_ge(var_p, h + 1)
                act.activation(quk[:, :], U[2][:, :], ACT.Sqrt, bias=epsc[:, 0:1]).then_inc(sd_r, 1)

            act.wait_ge(setup, 1)
            split_w(0)
            split_w(1)
            for s, (half, h) in enumerate(STAGES):
                if h is not None:
                    attention_in(h)
                norm_std(LN_OF_FFN[s])
                for b in range(NB):
                    act.activation(xhi[:, b, :], R[b][:, :], ACT.Copy).then_inc(xn_hi, 1)
                act.wait_ge(lg_sub, s + 1)
                act.activation(rt[:, 1].rearrange("p t e -> p (t e)"), rt[:, 0].rearrange("p t e -> p (t e)"), ACT.Exp).then_inc(p_exp, 1)
                for i in range(STEPS):
                    g = s * STEPS + i
                    if s == 0 and i == 0:
                        act.wait_ge(small_l, 16)
                    for f in range(FC):
                        n = g * FC + f
                        e = i % E
                        act.wait_ge(up, n + 1)
                        if n >= H32:
                            act.wait_ge(h_lo, n - H32 + 1)
                        act.activation(h32[:, n % H32, :], U[n % 3][:, :], ACT.Relu,
                                       bias=w(W_B1 + e * FC + f, 1)).then_inc(h_f, 1)
                    act.wait_ge(g_T, g + 1)
                    if g >= 2:
                        act.wait_ge(comb, g - 1)
                    act.activation(G[:, g % 2, :], R[i % 2][:, :], ACT.Copy).then_inc(g_c, 1)
                    if s == 0 and i + 2 < E:
                        split_w(i + 2)
                if h is not None:
                    attention_out(h)

        @block.vector
        def _(dve):
            count = [0]

            def link(ins):
                count[0] += 1
                ins.then_inc(dch, 1)
                dve.wait_ge(dch, count[0])

            def split_w(e):
                dve.wait_ge(w_in[e % 2], 16 * (e // 2 + 1))
                dve.wait_ge(whi_s, e + 1)
                dve.tensor_tensor(wlo[:, e].rearrange("p a f n -> p (a f n)"), wraw[:, e % 2, :],
                                  whi[:, e].rearrange("p a f n -> p (a f n)"), ALU.subtract).then_inc(wlo_s, 1)

            def norm(L):
                dve.wait_ge(ln_src, L + 1)
                for t in range(8):
                    last = dve.bn_stats(bst[:, t, :], U[t // 4][:, t % 4 * P:(t % 4 + 1) * P])
                link(last)
                for t in range(8):
                    last = dve.bn_aggr(mv[:, t, :], bst[:, t, :])
                last.then_inc(ln_var, 1)
                dve.wait_ge(ln_std, L + 1)
                link(dve.reciprocal(rstd[:, :], std[:, :]))
                for t in range(8):
                    last = dve.tensor_scalar(xnt[:, t, :], U[t // 4][:, t % 4 * P:(t % 4 + 1) * P],
                                             mv[:, t, 0:1], rstd[:, t:t + 1], ALU.subtract, ALU.mult)
                last.then_inc(ln_nrm, 1)

            def bc(x):
                return x.rearrange("p (t a) -> p t a", a=1).to_broadcast([P, 8, E])

            def route(s):
                dve.wait_ge(lg, s + 1)
                L = OB[:, 0:8 * E].rearrange("p (t e) -> p t e", e=E)
                link(dve.tensor_reduce(rs[:, 0], L, AX.X, ALU.max))
                dve.tensor_tensor(rt[:, 0], L, bc(rs[:, 0]), ALU.subtract).then_inc(lg_sub, 1)
                dve.wait_ge(p_exp, s + 1)
                link(dve.tensor_reduce(rs[:, 1], rt[:, 1], AX.X, ALU.add))
                link(dve.reciprocal(rs[:, 2], rs[:, 1]))
                link(dve.tensor_tensor(rt[:, 2], rt[:, 1], bc(rs[:, 2]), ALU.mult))
                pp, ch = rt[:, 2], []
                for n in range(2):
                    m = rs[:, 3 + n]
                    link(dve.tensor_reduce(m, pp, AX.X, ALU.max))
                    link(dve.tensor_tensor(rt[:, 3], pp, bc(m), ALU.is_equal))
                    link(dve.tensor_tensor(rt[:, 3], rt[:, 3], tie, ALU.mult))
                    link(dve.tensor_reduce(rs[:, 5], rt[:, 3], AX.X, ALU.max))
                    link(dve.tensor_tensor(rt[:, 4 + n], tie, bc(rs[:, 5]), ALU.is_equal))
                    if n == 0:
                        link(dve.scalar_tensor_tensor(out=flat(rt[:, 6]), in0=flat(rt[:, 4]), scalar=-2.0, in1=flat(pp), op0=ALU.mult, op1=ALU.add))
                        pp = rt[:, 6]
                link(dve.tensor_tensor(rt[:, 7], rt[:, 4], rt[:, 5], ALU.add))
                link(dve.tensor_tensor(rt[:, 3], rt[:, 7], rt[:, 2], ALU.mult))
                link(dve.scalar_tensor_tensor(out=rs[:, 6], in0=rs[:, 3], scalar=1e-9, in1=rs[:, 4], op0=ALU.add, op1=ALU.add))
                link(dve.reciprocal(rs[:, 7], rs[:, 6]))
                link(dve.tensor_scalar(rs[:, 5], rs[:, 7], 0.5, None, ALU.mult))
                dve.tensor_tensor(gate[:, :, :], rt[:, 3], bc(rs[:, 5]), ALU.mult).then_inc(gates, 1)

            def flat(x):
                return x.rearrange("p t e -> p (t e)")

            def combine(s, i):
                g = s * STEPS + i
                dve.wait_ge(down, (g + 1) * FC)
                dve.wait_ge(g_c, g + 1)
                if g >= 2:
                    dve.wait_ge(acc, g - 1)
                dve.scalar_tensor_tensor(out=gy[:, g % 2, :], in0=Y[g % 2][:, :], scalar=w(W_B2 + i % E, 1),
                                         in1=G[:, g % 2, :], op0=ALU.add, op1=ALU.mult).then_inc(comb, 1)

            def attention_in(h):
                norm(LN_OF_ATT[h])
                dve.wait_ge(xa_rdy, 2 * h + 2)
                if h == 0:
                    link(dve.memset(xa[:, :, 0:1], 0.0))
                link(dve.tensor_tensor(delta[:, :, :], xa[:, :, 0:NT], xa[:, :, 1:NT + 1], ALU.subtract))
                dve.scalar_tensor_tensor(out=xm[:, :, :], in0=delta[:, :, :], scalar=w(W_MU, 1),
                                         in1=xa[:, :, 1:NT + 1], op0=ALU.mult, op1=ALU.add).then_inc(xm_r, 1)
                for n in range(10):
                    i, b = divmod(n, NB)
                    dve.wait_ge(mus, 10 * h + n + 1)
                    if n >= TS:
                        dve.wait_ge(u_r, 10 * h + n - TS + 1)
                    dve.scalar_tensor_tensor(out=mix[:, n % TS, :], in0=MIXB[n % 8][:, :], scalar=w(W_XB + i, 1),
                                             in1=delta[:, b, :], op0=ALU.add, op1=ALU.mult).then_inc(mterm, 1)
                dve.wait_ge(ach, 7 * h + 2)
                dve.scalar_tensor_tensor(out=quk[:, :], in0=q[:, :], scalar=w(W_U, 1), in1=kk[:, :],
                                         op0=ALU.mult, op1=ALU.mult).then_inc(quk_r, 1)
                for g in range(NG):
                    dve.wait_ge(ach, 7 * h + 3 + g)
                    dve.tensor_tensor(vlo[:, g, :], Y[g][:, :], vhi[:, g, :], ALU.subtract).then_inc(vlo_r, 1)
                for g in range(NG):
                    dve.wait_ge(ach, 7 * h + 5 + g)
                    dve.scalar_tensor_tensor(out=sg[:, g, :], in0=sg[:, g, :], scalar=1.0, in1=R[g][:, :],
                                             op0=ALU.add, op1=ALU.mult).then_inc(sg_r, 1)
                dve.wait_ge(bet_c, h + 1)
                for g in range(NG):
                    dve.tensor_tensor(o[:, g, :], Y[g][:, :], aw, ALU.mult).then_inc(bv_r, 1)
                if h == 0:
                    dve.memset(S[:, :, 0:1], 0.0).then_inc(s_zero, 1)

            def scan(h, m):
                n = h * NV + m
                dve.wait_ge(vb, n + 1)
                if n >= 2:
                    dve.wait_ge(st_r, n - 1)
                dve.tensor_tensor(kv[:, n % 2, :], R[v_bank(m)][:, :], kk[:, :], ALU.mult).then_inc(kv_r, 1)
                if n >= SS:
                    dve.wait_ge(qs_r, n - SS + 1)
                init = 0.0
                if h == 1:
                    dve.wait_ge(seed, m + 1)
                    init = carry[:, m:m + 1]
                dve.wait_ge(kv_r, n + 1)
                dve.tensor_tensor_scan(S[:, n % SS, 1:NT + 1], dec[:, :], kv[:, n % 2, :], init,
                                       ALU.mult, ALU.add).then_inc(st_r, 1)

            def take_o(h, g):
                dve.wait_ge(red, h * 8 + 4 * g + 4)
                dve.tensor_tensor(o[:, g, :], OB[:, :], o[:, g, :], ALU.add).then_inc(o_r, 1)

            def attention_out(h):
                dve.wait_ge(sd_r, h + 1)
                link(dve.reciprocal(aw[:, :], quk[:, :]))
                for g in range(NG):
                    link(dve.tensor_tensor(z0[:, g, :], U[g][:, :], aw[:, :], ALU.mult))
                    link(dve.tensor_scalar(z0[:, g, :], z0[:, g, :], w(W_GW + g, 1), w(W_GB + g, 1), ALU.mult, ALU.add))
                    dve.scalar_tensor_tensor(out=o[:, g, :], in0=z0[:, g, :], scalar=0.5, in1=sg[:, g, :],
                                             op0=ALU.mult, op1=ALU.mult).then_inc(yo_r, 1)
                for b in range(NB):
                    dve.wait_ge(yp, NB * h + b + 1)
                    dve.tensor_tensor(xT[:, h, b, :], Y[b][:, :], xT[:, h, b, :], ALU.add).then_inc(x_att, 1)

            dve.memset(epsc[:, :], EPS).then_inc(setup, 1)
            dve.wait_ge(const_l, 16)
            for s, (half, h) in enumerate(STAGES):
                if h is not None:
                    attention_in(h)
                if s == 0:
                    split_w(0)
                norm(LN_OF_FFN[s])
                if s == 0:
                    split_w(1)
                    dve.wait_ge(small_l, 16)
                    link(dve.tensor_copy(rwh[:, 0, :], w(W_RT, E)))
                    link(dve.tensor_tensor(rwh[:, 1, :], w(W_RT, E), rwh[:, 0, :], ALU.subtract))
                for b in range(NB):
                    dve.wait_ge(xn_hi, 2 * s + b + 1)
                    dve.tensor_tensor(xlo[:, b, :], R[b][:, :], xhi[:, b, :], ALU.subtract).then_inc(xn_lo, 1)
                route(s)
                for i in range(STEPS):
                    for f in range(FC):
                        n = (s * STEPS + i) * FC + f
                        dve.wait_ge(h_hi, n + 1)
                        if n >= HS:
                            dve.wait_ge(down, n - HS + 1)
                        dve.tensor_tensor(hlo[:, n % HS, :], h32[:, n % H32, :], hhi[:, n % HS, :], ALU.subtract).then_inc(h_lo, 1)
                    if s == 0 and i + 2 < E:
                        split_w(i + 2)
                    if s == 0 and i == E:
                        dve.wait_ge(sel_l, 16)
                        dve.tensor_copy(sel[:, :, :].rearrange("p j n -> p (j n)"), sel_raw).then_inc(sel_r, 1)
                    if i >= 1:
                        combine(s, i - 1)
                    if h is not None:
                        if i >= 1:
                            scan(h, 2 * i - 2)
                            scan(h, 2 * i - 1)
                        if i == 10:
                            take_o(h, 0)
                if h is not None:
                    scan(h, 2 * STEPS - 2)
                    scan(h, 2 * STEPS - 1)
                combine(s, STEPS - 1)
                if h is not None:
                    take_o(h, 1)
                    attention_out(h)

        @block.gpsimd
        def _(pool):
            def split_h(s, i):
                for f in range(FC):
                    n = (s * STEPS + i) * FC + f
                    pool.wait_ge(h_f, n + 1)
                    if n >= HS:
                        pool.wait_ge(down, n - HS + 1)
                    pool.tensor_copy(hhi[:, n % HS, :], h32[:, n % H32, :]).then_inc(h_hi, 1)

            def add_y(s, half, i):
                b, g = i // E, s * STEPS + i
                pool.wait_ge(comb, g + 1)
                if g >= 1:
                    pool.wait_ge(acc, g)
                pool.tensor_tensor(xT[:, half, b, :], xT[:, half, b, :], gy[:, g % 2, :], ALU.add).then_inc(acc, 1)

            def read_state(h, m):
                n = h * NV + m
                pool.wait_ge(st_r, n + 1)
                if n >= QS:
                    pool.wait_ge(red, (n - QS) // 4 + 1)
                pool.tensor_tensor(qs[:, n % QS, :], q[:, :], S[:, n % SS, 0:NT], ALU.mult).then_inc(qs_r, 1)
                if h == 0:
                    pool.tensor_copy(carry[:, m:m + 1], S[:, n % SS, NT:NT + 1]).then_inc(pch, 1)

            def seed_state(m):
                n = NV + m
                pool.wait_ge(pch, m + 1)
                pool.wait_ge(qs_r, n - SS + 1)
                pool.tensor_copy(S[:, n % SS, 0:1], carry[:, m:m + 1]).then_inc(seed, 1)

            for s, (half, h) in enumerate(STAGES):
                if h is not None:
                    for n in range(10):
                        i, b = divmod(n, NB)
                        pool.wait_ge(mterm, 10 * h + n + 1)
                        pool.tensor_tensor(u[:, i, b, :], mix[:, n % TS, :], xa[:, b, 1:NT + 1], ALU.add).then_inc(u_r, 1)
                    if h == 0:
                        pool.wait_ge(u_r, 10)
                        pool.tensor_copy(xa[:, :, 0:1], xa[:, :, NT:NT + 1]).then_inc(xa_prev, 1)
                if h == 0:
                    pool.wait_ge(s_zero, 1)
                if h == 1:
                    pool.wait_ge(bv_r, 2 * NG)
                    for m in range(2):
                        seed_state(m)
                for i in range(STEPS):
                    split_h(s, i)
                    if i >= 1:
                        if h is not None:
                            for m in (2 * i - 2, 2 * i - 1):
                                read_state(h, m)
                                if h == 1 and m + 2 < NV:
                                    seed_state(m + 2)
                        add_y(s, half, i - 1)
                if h is not None:
                    for m in (2 * STEPS - 2, 2 * STEPS - 1):
                        read_state(h, m)
                add_y(s, half, STEPS - 1)


def order(m):
    g, r = divmod(m, VG)
    n, c = divmod(r, 4)
    return g, 4 * c + n


def v_bank(m):
    i, r = divmod(m, 2)
    return (i + 1) % 2 if r == 0 else i % 2


def lay_out(d):
    import numpy as np
    f = np.float32
    x = np.asarray(d["L0_attn_hidden_states"])
    xT = np.ascontiguousarray(x.reshape(NB, 2, NT, P).transpose(3, 1, 0, 2).reshape(P, 2 * NB * NT))
    w1, w2 = np.asarray(d["L0_ffn_w1"]), np.asarray(d["L0_ffn_w2"])
    wexp = np.zeros((P, E, 2, FC, P), f)
    wexp[:, :, 0] = w1.reshape(E, FC, P, P).transpose(3, 0, 1, 2)
    wexp[:, :, 1] = w2.reshape(E, P, FC, P).transpose(3, 0, 2, 1)
    s = np.zeros((P, W_ALL), f)
    g = {k[8:]: np.asarray(v) for k, v in d.items() if k.startswith("L0_attn_")}
    s[:, W_X1:W_X1 + 160] = g["W_x1"].T
    x2 = g["W_x2"].reshape(P, 5, 32).transpose(1, 2, 0)
    s[:, W_X2:W_X2 + P] = x2[:4].reshape(P, P)
    s[0:32, W_X2B:W_X2B + P] = x2[4]
    s[:, W_R:W_R + 64] = g["W_r"].T
    s[:, W_K:W_K + 64] = g["W_k"].T
    s[:, W_A:W_A + 64] = g["A_w"].T
    s[0:64, W_B:W_B + 64] = s[64:128, W_B:W_B + 64] = g["B_w"].T
    for at, name in ((W_V, "W_v"), (W_G, "W_g")):
        v = s[:, at:at + NG * NB * P].reshape(P, NG, NB, VG, NB, NH)
        src = g[name].reshape(NH, NG, VG, P).transpose(3, 1, 2, 0)
        for b in range(NB):
            v[:, :, b, :, b, :] = src
        s[:, at:at + NG * NB * P] = v.reshape(P, -1)
    v = np.zeros((VG, NB, NH, NG, NB, P), f)
    src = g["W_o"].reshape(P, NH, NG, VG).transpose(3, 1, 2, 0)
    for b in range(NB):
        v[:, b, :, :, b, :] = src
    s[:, W_O:W_O + NG * NB * P] = v.reshape(P, -1)
    s[:, W_RT:W_RT + E] = np.asarray(d["L0_ffn_router_w"]).T
    s[:, W_B1:W_B1 + E * FC] = np.asarray(d["L0_ffn_b1"]).reshape(E * FC, P).T
    s[:, W_B2:W_B2 + E] = np.asarray(d["L0_ffn_b2"]).T
    s[:, W_MU] = g["mu_x"]
    s[:, W_XB:W_XB + 5] = g["x_bias"].T
    s[:, W_BW] = np.tile(g["b_w"], NB)
    s[:, W_U] = np.tile(g["bonus"].reshape(-1), NB)
    for at, name in ((W_GW, "gn_weight"), (W_GB, "gn_bias")):
        src = g[name].reshape(NH, NG, VG).transpose(2, 0, 1)
        s[:, at:at + NG] = np.broadcast_to(src[:, None], (VG, NB, NH, NG)).reshape(P, NG)
    c = np.zeros((P, C_ALL), f)
    eye = np.eye(P, dtype=f)
    c[:, C_ID:C_ID + P] = eye
    bh_v, v_of = np.arange(P) % BH, np.arange(P) // BH
    bh_k = np.arange(P) // KD
    for j in range(VG):
        c[:, C_SEL + j * P:C_SEL + (j + 1) * P] = (v_of[:, None] == j) & (bh_v[:, None] == bh_k[None, :])
    for n in range(4):
        cols = np.arange(32)
        c[:, C_RED + 32 * n:C_RED + 32 * n + 32] = (cols[None, :] // BH == n) & (cols[None, :] % BH == bh_k[:, None])
    same = (bh_v[:, None] == bh_v[None, :]).astype(f) / NV
    c[:, C_CEN:C_CEN + P] = eye - same
    c[:, C_CEN + P:C_CEN + 2 * P] = -same
    c[:, C_AVG:C_AVG + P] = same
    c[:, C_BET:C_BET + P] = bh_k[:, None] == bh_v[None, :]
    c[:, C_TIE:C_TIE + 64] = np.tile(E - np.arange(E), 8)[None, :]
    return {"xT_dram": xT, "wexp_dram": wexp.reshape(P, -1), "small_dram": s, "const_dram": c}


def kernel(**inputs):
    import numpy as np
    import concourse.bacc as bacc
    from concourse.bass_utils import run_bass_kernel_spmd as run

    arrays = lay_out(inputs)
    nc = bacc.Bacc("TRN2", target_bir_lowering=False, num_devices=1)
    args = [nc.dram_tensor(n, a.shape, F32, kind="ExternalInput").ap() for n, a in arrays.items()]
    out = nc.dram_tensor("out_dram", (P, 2 * NB * NT), F32, kind="ExternalOutput").ap()
    program(nc, *args, out)
    r = run(nc, [arrays], core_ids=[0])
    y = r.results[0]["out_dram"].reshape(P, 2, NB, NT)
    return np.ascontiguousarray(y.transpose(2, 1, 3, 0).reshape(NB, 2 * NT, P))
```

```python
from contextlib import ExitStack

import concourse.bass as bass
from concourse import mybir

ALU = mybir.AluOpType
ACT = mybir.ActivationFunctionType
AX = mybir.AxisListType
F32 = mybir.dt.float32
F32R = mybir.dt.float32r

P = 128
NB = 2
NT = 512
E, FC = 8, 4
STEPS = NB * E
KD, NH, NV = 16, 4, 32
NG, VG = 2, 16
BH = NB * NH
EPS = 1e-5
STAGES = [(0, None), (1, 0), (0, 1), (1, None)]
LN_FFN = [0, 2, 6, 10]
LN_ATT = [4, 8]
MIX = [1, 0, 2, 3, 4]
T_AN, T_Z, T_MUS, T_PR, T_SC, T_PO = 6, 13, 17, 27, 35, 55
H32, HS, QS, SS = 4, 6, 8, 4

C_ID, C_RED, C_CEN, C_AVG, C_BET, C_TIE = 0, 128, 256, 512, 640, 768
C_SEL = C_TIE + 64
C_ALL = C_SEL + VG * P
W_X1, W_X2, W_X2B, W_R, W_K, W_A, W_B = 0, 160, 288, 416, 480, 544, 608
W_V = 672
W_G = W_V + NG * NB * P
W_O = W_G + NG * NB * P
W_RT = W_O + NG * NB * P
W_B1, W_B2 = W_RT + E, W_RT + E + E * FC
W_MU, W_XB = W_B2 + E, W_B2 + E + 1
W_BW, W_U, W_GW, W_GB = W_XB + 5, W_XB + 6, W_XB + 7, W_XB + 7 + NG
W_ALL = W_GB + NG


def program(nc, xT_in, wexp_in, small_in, const_in, out):
    with ExitStack() as ctx:
        def sb(name, shape, dt=F32):
            return ctx.enter_context(nc.sbuf_tensor(name, shape, dt))

        def sem(name):
            return ctx.enter_context(nc.semaphore(name))

        xT = sb("xT", [P, 2, NB, NT])
        pool_a = sb("pool_a", [P, 10 * NT])
        wraw = pool_a[:, 0:4 * NT].rearrange("p (a n) -> p a n", a=2)
        sel_raw = pool_a[:, 4 * NT:8 * NT]
        u = pool_a[:, :].rearrange("p (i b n) -> p i b n", i=5, b=NB)
        kv = pool_a[:, 0:2 * NT].rearrange("p (a n) -> p a n", a=2)
        o = pool_a[:, 2 * NT:4 * NT].rearrange("p (g n) -> p g n", g=NG)
        S = pool_a[:, 4 * NT:4 * NT + SS * (NT + 1)].rearrange("p (a n) -> p a n", a=SS)
        whi = sb("whi", [P, E, 2, FC, P], F32R)
        wlo = sb("wlo", [P, E, 2, FC, P], F32R)
        small = sb("small", [P, W_ALL])
        const = sb("const", [P, C_SEL])
        sel = sb("sel", [P, VG, P], F32R)
        rwh = sb("rwh", [P, 2, E], F32R)
        mv = sb("mv", [P, 8, 2])
        bst = sb("bst", [P, 8, 6])
        std = sb("std", [P, 8])
        rstd = sb("rstd", [P, 8])
        epsc = sb("epsc", [P, 1])
        xnt = sb("xnt", [P, 8, P])
        aw = xnt[:, 0:4, :].rearrange("p a n -> p (a n)")
        quk = xnt[:, 4:8, :].rearrange("p a n -> p (a n)")
        xhi = sb("xhi", [P, NB, NT], F32R)
        xlo = sb("xlo", [P, NB, NT], F32R)
        rt = sb("rt", [P, 8, 8, E])
        rs = sb("rs", [P, 8, 8])
        gate = sb("gate", [P, 8, E])
        G = sb("G", [P, 2, NT])
        h32 = sb("h32", [P, H32, NT])
        hhi = sb("hhi", [P, HS, NT], F32R)
        hlo = sb("hlo", [P, HS, NT], F32R)
        gy = sb("gy", [P, 2, NT])
        xa = sb("xa", [P, NB, NT + 1])
        qs = sb("qs", [P, QS, NT])
        delta, xm, z0, z1 = qs[:, 0:2, :], qs[:, 2:4, :], qs[:, 4:6, :], qs[0:64, 6, :]
        q = sb("q", [P, NT])
        kk = sb("kk", [P, NT])
        dec = sb("dec", [P, NT])
        vhi = sb("vhi", [P, NG, NT], F32R)
        vlo = sb("vlo", [P, NG, NT], F32R)
        sg = sb("sg", [P, NG, NT])
        carry = sb("carry", [P, NV])

        U = [ctx.enter_context(nc.psum_tensor(f"U{i}", [P, NT], F32)) for i in range(3)]
        Y = [ctx.enter_context(nc.psum_tensor(f"Y{i}", [P, NT], F32)) for i in range(2)]
        R = [ctx.enter_context(nc.psum_tensor(f"R{i}", [P, NT], F32)) for i in range(2)]
        OB = ctx.enter_context(nc.psum_tensor("OB", [P, NT], F32))
        A = R + [OB]

        ident = const[:, C_ID:C_ID + P]
        tie = const[:, C_TIE:C_TIE + 64].rearrange("p (t e) -> p t e", e=E)

        def w(at, n, rows=slice(0, P)):
            return small[rows, at:at + n]

        x_in, w_in, small_l, const_l, sel_l = sem("x_in"), [sem("w_in0"), sem("w_in1")], sem("small_in"), sem("const_in"), sem("sel_in")
        whi_s, wlo_s, sel_r, rw_r, setup, out_done = sem("w_hi"), sem("w_lo"), sem("sel_r"), sem("rw_r"), sem("setup"), sem("out_done")
        ln_src, ln_var, ln_std, ln_nrm, ln_T = (sem(n) for n in ("ln_src", "ln_var", "ln_std", "ln_nrm", "ln_T"))
        xn_hi, xn_lo, xa_rdy = sem("xn_hi"), sem("xn_lo"), sem("xa_rdy")
        lg, lg_sub, p_exp, gates = sem("logits"), sem("logits_sub"), sem("p_exp"), sem("gates")
        up, h_f, h_lo, down = sem("up"), sem("h_f"), sem("h_lo"), sem("down")
        g_T, g_c, comb, acc = sem("g_T"), sem("g_c"), sem("comb"), sem("acc")
        dch, pch = sem("dve_chain"), sem("carry_r")
        xa_zero, xa_prev, xm_r, z_p, z_r, mus, mterm, u_r = (sem(n) for n in ("xa_zero", "xa_prev", "xm_r", "z_p", "z_r", "mus", "mterm", "u_r"))
        pr, aw_r, q_r, k_r, quk_r, bet, bet_c, bv_r = (sem(n) for n in ("proj", "aw_r", "q_r", "k_r", "quk_r", "beta", "beta_c", "bv_r"))
        vhi_r, vlo_r, sg_t, sg_r, wb_r, e_r, dec_r = (sem(n) for n in ("vhi_r", "vlo_r", "sg_t", "sg_r", "wb_r", "e_r", "dec_r"))
        vb, kv_r, st_r, qs_r, red, o_r, seed, s_zero = (sem(n) for n in ("vb", "kv_r", "st_r", "qs_r", "red", "o_r", "seed", "s_zero"))
        cen, sq_r, var_p, sd_r, yo_r, yp, x_att = (sem(n) for n in ("cen", "sq_r", "var_p", "sd_r", "yo_r", "yp", "x_att"))

        block = ctx.enter_context(nc.Block())

        @block.sync
        def _(sp):
            xi = xT_in.rearrange("p (h b n) -> p h b n", h=2, b=NB)
            sp.dma_start(xT[:, 0, :, :], xi[:, 0]).then_inc(x_in, 16)
            sp.dma_start(const[:, :], const_in[:, 0:C_SEL]).then_inc(const_l, 16)
            for e in range(E):
                if e >= 2:
                    sp.wait_ge(whi_s, e - 1)
                    sp.wait_ge(wlo_s, e - 1)
                sp.dma_start(wraw[:, e % 2, :], wexp_in[:, e * 2 * NT:(e + 1) * 2 * NT]).then_inc(w_in[e % 2], 16)
                if e == 1:
                    sp.dma_start(small[:, :], small_in).then_inc(small_l, 16)
            sp.dma_start(sel_raw, const_in[:, C_SEL:C_ALL]).then_inc(sel_l, 16)
            sp.wait_ge(x_in, 16)
            sp.dma_start(xT[:, 1, :, :], xi[:, 1]).then_inc(x_in, 16)
            ov = out.rearrange("p (h b n) -> p h b n", h=2, b=NB)
            for s in (2, 3):
                for b in range(NB):
                    sp.wait_ge(acc, s * STEPS + (b + 1) * E)
                    sp.dma_start(ov[:, s - 2, b], xT[:, s - 2, b, :]).then_inc(out_done, 16)
            sp.wait_ge(out_done, 64)

        @block.tensor
        def _(pe):
            mm = pe.matmul

            def ffn_up(s, i, f):
                b, e = divmod(i, E)
                g = s * STEPS + i
                n = g * FC + f
                item = 5 * g + f
                if item >= 3:
                    wait_u(item - 3)
                if f == 0 and i % E == 0:
                    pe.wait_ge(xn_hi, 2 * s + b + 1)
                    pe.wait_ge(xn_lo, 2 * s + b + 1)
                if s == 0 and f == 0 and b == 0:
                    pe.wait_ge(whi_s, e + 1)
                    pe.wait_ge(wlo_s, e + 1)
                dst = U[item % 3][:, :]
                mm(dst, wlo[:, e, 0, f, :], xhi[:, b, :], start=True, stop=False)
                mm(dst, whi[:, e, 0, f, :], xlo[:, b, :], start=False, stop=False)
                mm(dst, whi[:, e, 0, f, :], xhi[:, b, :], start=False, stop=True).then_inc(up, 1)

            def wait_u(item):
                g, f = divmod(item, 5)
                if f < FC:
                    pe.wait_ge(h_f, g * FC + f + 1)
                else:
                    pe.wait_ge(g_c, g + 1)

            def ffn_down(g, f):
                e, n = g % E, g * FC + f
                if f == 0 and g >= 2:
                    pe.wait_ge(comb, g - 1)
                pe.wait_ge(h_lo, n + 1)
                dst = Y[g % 2][:, :]
                mm(dst, wlo[:, e, 1, f, :], hhi[:, n % HS, :], start=(f == 0), stop=False)
                mm(dst, whi[:, e, 1, f, :], hlo[:, n % HS, :], start=False, stop=False)
                mm(dst, whi[:, e, 1, f, :], hhi[:, n % HS, :], start=False, stop=(f == FC - 1)).then_inc(down, 1)

            def gates_out(s, i):
                b, e = divmod(i, E)
                item = 5 * (s * STEPS + i) + FC
                wait_u(item - 3)
                pe.wait_ge(gates, 2 * s + b + 1)
                for t in range(4):
                    last = pe.transpose(U[item % 3][:, t * P:(t + 1) * P], gate[:, 4 * b + t, e:e + 1].to_broadcast([P, P]), ident)
                last.then_inc(g_T, 1)

            def to_tokens(bank, half, b):
                for t in range(4):
                    last = pe.transpose(A[bank][:, t * P:(t + 1) * P], xT[:, half, b, t * P:(t + 1) * P], ident)
                last.then_inc(ln_src, 1)

            def to_channels(k, bank):
                pe.wait_ge(ln_nrm, k + 1)
                for t in range(4):
                    last = pe.transpose(A[bank][:, t * P:(t + 1) * P], xnt[:, k % 2 * 4 + t, :], ident)
                last.then_inc(ln_T, 1)

            def prep_src(s, b):
                if s == 1:
                    pe.wait_ge(x_in, 32)
                    pe.wait_ge(xn_lo, b + 1)
                if s >= 2:
                    pe.wait_ge(yo_r, NG * (s - 1))
                    pe.wait_ge(x_att, NB * (s - 1) if b else NB * (s - 2) + 1)
                to_tokens(1 - b, STAGES[s][0], b)

            def logits(s, b):
                pe.wait_ge(xn_hi, 2 * s + b + 1)
                pe.wait_ge(xn_lo, 2 * s + b + 1)
                if s == 0:
                    pe.wait_ge(rw_r, 1)
                if 2 * s + b > 0:
                    pe.wait_ge(lg_sub, 2 * s + b)
                if s >= 2:
                    pe.wait_ge(x_att, NB * (s - 2) + 1)
                for t in range(4):
                    dst = A[2][:, (4 * b + t) * E:(4 * b + t + 1) * E]
                    for n, (x, r) in enumerate(((xlo, 1), (xlo, 0), (xhi, 1), (xhi, 0))):
                        last = mm(dst, x[:, b, t * P:(t + 1) * P], rwh[:, r, :], start=(n == 0), stop=(n == 3))
                last.then_inc(lg, 1)

            def z_of(h, n):
                if n < NB:
                    if n == 0:
                        pe.wait_ge(xm_r, h + 1)
                    else:
                        pe.wait_ge(xa_rdy, 2 * h + 1)
                    mm(A[1 + n][:, :], w(W_X1, P), xm[:, n, :], start=True, stop=True).then_inc(z_p, 1)
                else:
                    pe.wait_ge(xa_rdy, 2 * h + 2)
                    for b in range(NB):
                        last = mm(A[0][32 * b:32 * b + 32, :], w(W_X1 + P, 32), xm[:, b, :], start=True, stop=True)
                    last.then_inc(z_p, 1)

            def mus_of(h, n):
                i, b = MIX[n // NB], n % NB
                if n < 3:
                    pe.wait_ge(z_r, 3 * h + n + 1)
                else:
                    pe.wait_ge(mterm, 10 * h + n - 2)
                if i < 4:
                    mm(A[(n + 1) % 3][:, :], w(W_X2, P, slice(32 * i, 32 * i + 32)), z0[32 * i:32 * i + 32, b, :],
                       start=True, stop=True).then_inc(mus, 1)
                else:
                    mm(A[(n + 1) % 3][:, :], w(W_X2B, P, slice(32 * b, 32 * b + 32)), z1[32 * b:32 * b + 32, :],
                       start=True, stop=True).then_inc(mus, 1)

            def proj_bk(h, bank, at, i):
                for b in range(NB):
                    last = mm(A[bank][64 * b:64 * b + 64, :], w(at, 64), u[:, i, b, :], start=True, stop=True)
                last.then_inc(pr, 1)

            def proj_vbh(h, bank, at, i, g):
                for b in range(NB):
                    last = mm(A[bank][:, :], w(at + (g * NB + b) * P, P), u[:, i, b, :], start=(b == 0), stop=(b == 1))
                last.then_inc(pr, 1)

            def v_spread(h, m):
                g, j = order(m)
                if m >= 2:
                    pe.wait_ge(kv_r, h * NV + m - 1)
                else:
                    pe.wait_ge(sg_r, NG * h + (2 if m == 0 else 1))
                    pe.wait_ge(sel_r, 1)
                    pe.wait_ge(vlo_r, NG * (h + 1))
                mm(A[m % 2][:, :], sel[:, j, :], vlo[:, g, :], start=True, stop=False)
                mm(A[m % 2][:, :], sel[:, j, :], vhi[:, g, :], start=False, stop=True).then_inc(vb, 1)

            def reduce(h, n):
                pe.wait_ge(qs_r, h * NV + 4 * n + 4)
                if n == 0:
                    pe.wait_ge(e_r, h + 1)
                if n == 4:
                    pe.wait_ge(o_r, h * NG + 1)
                c0 = C_RED + 32 * (n % 4)
                for c in range(4):
                    last = mm(A[2][32 * c:32 * c + 32, :], const[:, c0:c0 + 32], qs[:, (4 * n + c) % QS, :],
                              start=(n % 4 == 0), stop=(n % 4 == 3))
                last.then_inc(red, 1)

            def centre(h):
                pe.wait_ge(o_r, NG * (h + 1))
                for g in range(NG):
                    for g2 in range(NG):
                        c0 = C_CEN if g == g2 else C_CEN + P
                        last = mm(A[g][:, :], const[:, c0:c0 + P], o[:, g2, :], start=(g2 == 0), stop=(g2 == 1))
                    last.then_inc(cen, 1)

            def variance(h):
                pe.wait_ge(sq_r, NG * (h + 1))
                for g in range(NG):
                    last = mm(A[2][:, :], const[:, C_AVG:C_AVG + P], xm[:, g, :], start=(g == 0), stop=(g == 1))
                last.then_inc(var_p, 1)

            def out_proj(h):
                pe.wait_ge(yo_r, NG * (h + 1))
                for b in range(NB):
                    for g in range(NG):
                        last = mm(A[2 * (1 - b)][:, :], w(W_O + (g * NB + b) * P, P), o[:, g, :], start=(g == 0), stop=(g == 1))
                    last.then_inc(yp, 1)

            def beside(s, h, t):
                if t == 0 and s > 0:
                    logits(s, 0)
                if t == 1 and s > 0:
                    logits(s, 1)
                if s == 0:
                    if t == 40:
                        prep_src(1, 0)
                    if t == 44:
                        to_channels(LN_FFN[1], 1)
                    if t == 52:
                        prep_src(1, 1)
                    if t == 56:
                        to_channels(LN_FFN[1] + 1, 0)
                if h is None:
                    return
                k = LN_ATT[h]
                if t == T_AN:
                    for b in range(NB):
                        pe.wait_ge(acc, h * STEPS + (b + 1) * E)
                        pe.wait_ge(xn_lo, 2 * s + 2)
                        to_tokens(b, h, b)
                if t == T_AN + 4:
                    pe.wait_ge(gates, 2 * s + 2)
                    to_channels(k, 2)
                    to_channels(k + 1, 0)
                if T_Z <= t < T_Z + 3:
                    z_of(h, t - T_Z)
                if T_MUS <= t < T_MUS + 10:
                    mus_of(h, t - T_MUS)
                if t == T_PR:
                    pe.wait_ge(mterm, 10 * h + 8)
                    pe.wait_ge(u_r, 10 * h + 2)
                    proj_bk(h, 2, W_A, 1)
                if t == T_PR + 1:
                    pe.wait_ge(mterm, 10 * h + 9)
                    pe.wait_ge(u_r, 10 * h + 4)
                    proj_bk(h, 0, W_R, 0)
                    pe.wait_ge(mterm, 10 * h + 10)
                    pe.wait_ge(u_r, 10 * h + 6)
                    proj_bk(h, 1, W_K, 2)
                if t == T_PR + 2:
                    pe.wait_ge(aw_r, h + 1)
                    pe.wait_ge(u_r, 10 * h + 8)
                    proj_vbh(h, 2, W_V, 3, 0)
                if t == T_PR + 3:
                    pe.wait_ge(q_r, h + 1)
                    proj_vbh(h, 0, W_V, 3, 1)
                if t == T_PR + 4:
                    pe.wait_ge(quk_r, h + 1)
                    mm(A[1][:, :], const[:, C_BET:C_BET + P], quk[:, :], start=True, stop=True).then_inc(bet, 1)
                if t == T_PR + 5:
                    pe.wait_ge(bet_c, h + 1)
                    pe.wait_ge(u_r, 10 * h + 10)
                    proj_vbh(h, 1, W_G, 4, 0)
                if t == T_PR + 6:
                    pe.wait_ge(bv_r, NG * h + 1)
                    for b in range(NB):
                        hb = slice(64 * b, 64 * b + 64)
                        last = mm(A[2][hb, :], w(W_B, 64, hb), aw[hb, :], start=True, stop=True)
                    last.then_inc(wb_r, 1)
                if t == T_PR + 7:
                    pe.wait_ge(bv_r, NG * h + 2)
                    proj_vbh(h, 0, W_G, 4, 1)
                if T_SC <= t < T_SC + NV // 2:
                    v_spread(h, 2 * (t - T_SC))
                    v_spread(h, 2 * (t - T_SC) + 1)
                if T_SC + 3 <= t < T_SC + 3 + NV // 2 and (t - T_SC - 3) % 2 == 0:
                    reduce(h, (t - T_SC - 3) // 2)
                if t == T_PO:
                    centre(h)
                if t == T_PO + 2:
                    variance(h)
                if t == T_PO + 6:
                    out_proj(h)
                    for b in range(NB):
                        prep_src(s + 1, b)

            pe.wait_ge(const_l, 16)
            pe.wait_ge(x_in, 16)
            for b in range(NB):
                prep_src(0, b)
            for b in range(NB):
                to_channels(b, 1 - b)
            for b in range(NB):
                logits(0, b)
            for s, (half, h) in enumerate(STAGES):
                for i in range(STEPS):
                    g = s * STEPS + i
                    for f in range(FC):
                        ffn_up(s, i, f)
                        if g > 0:
                            ffn_down(g - 1, f)
                        beside(s, h, 4 * i + f)
                    gates_out(s, i)
                if h is not None:
                    for b in range(NB):
                        to_channels(LN_FFN[s + 1] + b, 1 - b)
            for f in range(FC):
                ffn_down(4 * STEPS - 1, f)

        @block.scalar
        def _(act):
            def split_w(e):
                act.wait_ge(w_in[e % 2], 16 * (e // 2 + 1))
                act.activation(whi[:, e].rearrange("p a f n -> p (a f n)"), wraw[:, e % 2, :], ACT.Copy).then_inc(whi_s, 1)

            def deviation(k):
                act.wait_ge(ln_var, k + 1)
                v = slice(k % 2 * 4, k % 2 * 4 + 4)
                act.activation(std[:, v], mv[:, v, 1], ACT.Sqrt, bias=epsc[:, 0:1]).then_inc(ln_std, 1)

            def ffn_hi(s, b):
                act.wait_ge(ln_T, LN_FFN[s] + b + 1)
                if s >= 1:
                    act.wait_ge(up, ((s - 1) * STEPS + (b + 1) * E) * FC)
                act.activation(xhi[:, b, :], A[1 - b][:, :], ACT.Copy).then_inc(xn_hi, 1)

            def experts_exp(s, b):
                act.wait_ge(lg_sub, 2 * s + b + 1)
                act.activation(rt[:, 1, 0:4].rearrange("p t e -> p (t e)"), rt[:, 0, 0:4].rearrange("p t e -> p (t e)"),
                               ACT.Exp).then_inc(p_exp, 1)

            def relu(s, i, f):
                g = s * STEPS + i
                n = g * FC + f
                act.wait_ge(up, n + 1)
                if n >= H32:
                    act.wait_ge(h_lo, n - H32 + 1)
                if n >= HS:
                    act.wait_ge(down, n - HS + 1)
                bias = w(W_B1 + i % E * FC + f, 1)
                src = U[(5 * g + f) % 3][:, :]
                act.activation(h32[:, n % H32, :], src, ACT.Relu, bias=bias)
                act.activation(hhi[:, n % HS, :], src, ACT.Relu, bias=bias).then_inc(h_f, 1)

            def gate_copy(s, i):
                g = s * STEPS + i
                act.wait_ge(g_T, g + 1)
                if g >= 2:
                    act.wait_ge(comb, g - 1)
                act.activation(G[:, g % 2, :], U[(5 * g + FC) % 3][:, :], ACT.Copy).then_inc(g_c, 1)

            def beside(s, h, t):
                if s > 0 and t == 1:
                    experts_exp(s, 0)
                if s > 0 and t == 2:
                    experts_exp(s, 1)
                if s == 0:
                    if t == 41:
                        deviation(LN_FFN[1])
                    if t == 45:
                        ffn_hi(1, 0)
                    if t == 53:
                        deviation(LN_FFN[1] + 1)
                    if t == 63:
                        ffn_hi(1, 1)
                if h is None:
                    return
                k = LN_ATT[h]
                if t == T_AN + 1:
                    deviation(k)
                    deviation(k + 1)
                if t == T_AN + 4:
                    for b in range(NB):
                        act.wait_ge(ln_T, k + b + 1)
                        if h == 1 and b == 0:
                            act.wait_ge(xa_prev, 1)
                        act.activation(xa[:, b, 1:NT + 1], A[(2, 0)[b]][:, :], ACT.Copy).then_inc(xa_rdy, 1)
                if T_Z + 1 <= t < T_Z + 3:
                    b = t - T_Z - 1
                    act.wait_ge(z_p, 3 * h + b + 1)
                    act.activation(z0[:, b, :], A[1 + b][:, :], ACT.Tanh).then_inc(z_r, 1)
                if t == T_Z + 3:
                    act.wait_ge(z_p, 3 * h + 3)
                    act.activation(z1, A[0][0:64, :], ACT.Tanh).then_inc(z_r, 1)
                if t == T_PR:
                    act.wait_ge(pr, 7 * h + 1)
                    act.activation(aw, A[2][:, :], ACT.Tanh).then_inc(aw_r, 1)
                if t == T_PR + 1:
                    act.wait_ge(pr, 7 * h + 2)
                    act.activation(q[:, :], A[0][:, :], ACT.Copy).then_inc(q_r, 1)
                    act.wait_ge(pr, 7 * h + 3)
                    act.activation(kk[:, :], A[1][:, :], ACT.Copy).then_inc(k_r, 1)
                if T_PR + 2 <= t < T_PR + 4:
                    g = t - T_PR - 2
                    act.wait_ge(pr, 7 * h + 4 + g)
                    act.activation(vhi[:, g, :], A[2 - 2 * g][:, :], ACT.Copy).then_inc(vhi_r, 1)
                if t == T_PR + 4:
                    act.wait_ge(bet, h + 1)
                    act.activation(quk, A[1][:, :], ACT.Copy).then_inc(bet_c, 1)
                if t == T_PR + 5:
                    act.wait_ge(pr, 7 * h + 6)
                    act.activation(sg[:, 0, :], A[1][:, :], ACT.Tanh, scale=0.5).then_inc(sg_t, 1)
                if t == T_PR + 6:
                    act.wait_ge(wb_r, h + 1)
                    act.activation(dec[:, :], A[2][:, :], ACT.Exp, bias=w(W_BW, 1)).then_inc(e_r, 1)
                if t == T_PR + 7:
                    act.wait_ge(pr, 7 * h + 7)
                    act.activation(sg[:, 1, :], A[0][:, :], ACT.Tanh, scale=0.5).then_inc(sg_t, 1)
                    act.wait_ge(e_r, h + 1)
                    act.activation(dec[:, :], dec[:, :], ACT.Exp, scale=-1.0).then_inc(dec_r, 1)
                if t == T_PO:
                    for g in range(NG):
                        act.wait_ge(cen, NG * h + g + 1)
                        act.activation(xm[:, g, :], A[g][:, :], ACT.Square).then_inc(sq_r, 1)
                if t == T_PO + 3:
                    act.wait_ge(var_p, h + 1)
                    act.activation(quk, A[2][:, :], ACT.Sqrt, bias=epsc[:, 0:1]).then_inc(sd_r, 1)

            act.wait_ge(setup, 1)
            deviation(0)
            deviation(1)
            split_w(0)
            ffn_hi(0, 0)
            split_w(1)
            ffn_hi(0, 1)
            experts_exp(0, 0)
            experts_exp(0, 1)
            act.wait_ge(small_l, 16)
            for s, (half, h) in enumerate(STAGES):
                for i in range(STEPS):
                    for f in range(FC):
                        relu(s, i, f)
                        beside(s, h, 4 * i + f)
                    gate_copy(s, i)
                    if s == 0 and i + 2 < E:
                        split_w(i + 2)
                if h is not None:
                    for b in range(NB):
                        deviation(LN_FFN[s + 1] + b)
                    for b in range(NB):
                        ffn_hi(s + 1, b)

        @block.vector
        def _(dve):
            count = [0]

            def link(ins):
                count[0] += 1
                ins.then_inc(dch, 1)
                dve.wait_ge(dch, count[0])

            def split_w(e):
                dve.wait_ge(w_in[e % 2], 16 * (e // 2 + 1))
                dve.wait_ge(whi_s, e + 1)
                dve.tensor_tensor(wlo[:, e].rearrange("p a f n -> p (a f n)"), wraw[:, e % 2, :],
                                  whi[:, e].rearrange("p a f n -> p (a f n)"), ALU.subtract).then_inc(wlo_s, 1)

            def stats(k, bank):
                dve.wait_ge(ln_src, k + 1)
                t0 = k % 2 * 4
                for t in range(4):
                    last = dve.bn_stats(bst[:, t0 + t, :], A[bank][:, t * P:(t + 1) * P])
                link(last)
                for t in range(4):
                    last = dve.bn_aggr(mv[:, t0 + t, :], bst[:, t0 + t, :])
                last.then_inc(ln_var, 1)

            def normalise(k, bank):
                dve.wait_ge(ln_std, k + 1)
                t0 = k % 2 * 4
                link(dve.reciprocal(rstd[:, t0:t0 + 4], std[:, t0:t0 + 4]))
                for t in range(4):
                    last = dve.tensor_scalar(xnt[:, t0 + t, :], A[bank][:, t * P:(t + 1) * P],
                                             mv[:, t0 + t, 0:1], rstd[:, t0 + t:t0 + t + 1], ALU.subtract, ALU.mult)
                last.then_inc(ln_nrm, 1)

            def ffn_lo(s, b):
                dve.wait_ge(xn_hi, 2 * s + b + 1)
                dve.tensor_tensor(xlo[:, b, :], A[1 - b][:, :], xhi[:, b, :], ALU.subtract).then_inc(xn_lo, 1)

            def bc(x):
                return x.rearrange("p (t a) -> p t a", a=1).to_broadcast([P, 4, E])

            def flat(x):
                return x.rearrange("p t e -> p (t e)")

            def route_a(s, b):
                dve.wait_ge(lg, 2 * s + b + 1)
                L = A[2][:, 4 * b * E:4 * (b + 1) * E].rearrange("p (t e) -> p t e", e=E)
                link(dve.tensor_reduce(rs[:, 0, 0:4], L, AX.X, ALU.max))
                dve.tensor_tensor(rt[:, 0, 0:4], L, bc(rs[:, 0, 0:4]), ALU.subtract).then_inc(lg_sub, 1)

            def route_b(s, b):
                def r(n):
                    return rs[:, n, 0:4]

                def m(n):
                    return rt[:, n, 0:4]

                tie4 = tie[:, 0:4]
                dve.wait_ge(p_exp, 2 * s + b + 1)
                link(dve.tensor_reduce(r(1), m(1), AX.X, ALU.add))
                link(dve.reciprocal(r(2), r(1)))
                link(dve.tensor_tensor(m(2), m(1), bc(r(2)), ALU.mult))
                pp = m(2)
                for n in range(2):
                    top = r(3 + n)
                    link(dve.tensor_reduce(top, pp, AX.X, ALU.max))
                    link(dve.tensor_tensor(m(3), pp, bc(top), ALU.is_equal))
                    link(dve.tensor_tensor(m(3), m(3), tie4, ALU.mult))
                    link(dve.tensor_reduce(r(5), m(3), AX.X, ALU.max))
                    link(dve.tensor_tensor(m(4 + n), tie4, bc(r(5)), ALU.is_equal))
                    if n == 0:
                        link(dve.scalar_tensor_tensor(out=flat(m(6)), in0=flat(m(4)), scalar=-2.0, in1=flat(pp),
                                                      op0=ALU.mult, op1=ALU.add))
                        pp = m(6)
                link(dve.tensor_tensor(m(7), m(4), m(5), ALU.add))
                link(dve.tensor_tensor(m(3), m(7), m(2), ALU.mult))
                link(dve.scalar_tensor_tensor(out=r(6), in0=r(3), scalar=1e-9, in1=r(4), op0=ALU.add, op1=ALU.add))
                link(dve.reciprocal(r(7), r(6)))
                link(dve.tensor_scalar(r(5), r(7), 0.5, None, ALU.mult))
                if s >= 1:
                    dve.wait_ge(g_T, (s - 1) * STEPS + (b + 1) * E)
                dve.tensor_tensor(gate[:, 4 * b:4 * b + 4, :], m(3), bc(r(5)), ALU.mult).then_inc(gates, 1)

            def split_h(n):
                dve.wait_ge(h_f, n + 1)
                dve.tensor_tensor(hlo[:, n % HS, :], h32[:, n % H32, :], hhi[:, n % HS, :], ALU.subtract).then_inc(h_lo, 1)

            def combine(g):
                dve.wait_ge(down, (g + 1) * FC)
                dve.wait_ge(g_c, g + 1)
                if g >= 2:
                    dve.wait_ge(acc, g - 1)
                dve.scalar_tensor_tensor(out=gy[:, g % 2, :], in0=Y[g % 2][:, :], scalar=w(W_B2 + g % E, 1),
                                         in1=G[:, g % 2, :], op0=ALU.add, op1=ALU.mult).then_inc(comb, 1)

            def scan(h, m):
                n = h * NV + m
                dve.wait_ge(vb, n + 1)
                dve.tensor_tensor(kv[:, n % 2, :], A[m % 2][:, :], kk[:, :], ALU.mult).then_inc(kv_r, 1)
                if n >= SS:
                    dve.wait_ge(qs_r, n - SS + 1)
                if m == 0:
                    dve.wait_ge(dec_r, h + 1)
                    if h == 1:
                        dve.wait_ge(pch, NV)
                dve.wait_ge(kv_r, n + 1)
                dve.tensor_tensor_scan(S[:, n % SS, 1:NT + 1], dec[:, :], kv[:, n % 2, :], carry[:, m:m + 1] if h else 0.0,
                                       ALU.mult, ALU.add).then_inc(st_r, 1)

            def take_o(h, g):
                dve.wait_ge(red, h * 8 + 4 * g + 4)
                dve.tensor_tensor(o[:, g, :], A[2][:, :], o[:, g, :], ALU.add).then_inc(o_r, 1)

            def group_norm(h):
                dve.wait_ge(sd_r, h + 1)
                link(dve.reciprocal(aw, quk))
                for g in range(NG):
                    link(dve.tensor_tensor(z0[:, g, :], A[g][:, :], aw, ALU.mult))
                for g in range(NG):
                    link(dve.tensor_scalar(z0[:, g, :], z0[:, g, :], w(W_GW + g, 1), w(W_GB + g, 1), ALU.mult, ALU.add))
                for g in range(NG):
                    dve.scalar_tensor_tensor(out=o[:, g, :], in0=z0[:, g, :], scalar=0.5, in1=sg[:, g, :],
                                             op0=ALU.mult, op1=ALU.mult).then_inc(yo_r, 1)

            def beside(s, h, t):
                if s > 0 and t == 0:
                    route_a(s, 0)
                if s > 0 and t == 1:
                    route_a2(s)
                if s > 0 and t == 2:
                    route_b(s, 1)
                if s == 0:
                    if t == 40:
                        stats(LN_FFN[1], 1)
                    if t == 42:
                        normalise(LN_FFN[1], 1)
                    if t == 46:
                        ffn_lo(1, 0)
                    if t == 52:
                        stats(LN_FFN[1] + 1, 0)
                    if t == 54:
                        normalise(LN_FFN[1] + 1, 0)
                    if t == 32:
                        dve.wait_ge(sel_l, 16)
                        dve.tensor_copy(sel[:, :, :].rearrange("p j n -> p (j n)"), sel_raw).then_inc(sel_r, 1)
                if h is None:
                    return
                k = LN_ATT[h]
                if t == T_AN:
                    stats(k, 0)
                    stats(k + 1, 1)
                if t == T_AN + 2:
                    normalise(k, 0)
                    normalise(k + 1, 1)
                if t == T_AN + 5:
                    dve.wait_ge(xa_rdy, 2 * h + 2)
                    if h == 0:
                        link(dve.memset(xa[:, :, 0:1], 0.0))
                    link(dve.tensor_tensor(delta[:, :, :], xa[:, :, 0:NT], xa[:, :, 1:NT + 1], ALU.subtract))
                    dve.scalar_tensor_tensor(out=xm[:, :, :], in0=delta[:, :, :], scalar=w(W_MU, 1),
                                             in1=xa[:, :, 1:NT + 1], op0=ALU.mult, op1=ALU.add).then_inc(xm_r, 1)
                if T_MUS <= t < T_MUS + 10:
                    n = t - T_MUS
                    i, b = MIX[n // NB], n % NB
                    dve.wait_ge(mus, 10 * h + n + 1)
                    dve.scalar_tensor_tensor(out=u[:, i, b, :], in0=A[(n + 1) % 3][:, :], scalar=w(W_XB + i, 1),
                                             in1=delta[:, b, :], op0=ALU.add, op1=ALU.mult).then_inc(mterm, 1)
                if t == T_PR + 2:
                    dve.wait_ge(q_r, h + 1)
                    dve.wait_ge(k_r, h + 1)
                    dve.scalar_tensor_tensor(out=quk, in0=q[:, :], scalar=w(W_U, 1), in1=kk[:, :],
                                             op0=ALU.mult, op1=ALU.mult).then_inc(quk_r, 1)
                if t == T_PR + 4:
                    for g in range(NG):
                        dve.wait_ge(vhi_r, NG * h + g + 1)
                        dve.tensor_tensor(vlo[:, g, :], A[2 - 2 * g][:, :], vhi[:, g, :], ALU.subtract).then_inc(vlo_r, 1)
                if t == T_PR + 5:
                    dve.wait_ge(bet_c, h + 1)
                    for g in range(NG):
                        dve.tensor_tensor(o[:, g, :], A[2 - 2 * g][:, :], quk, ALU.mult).then_inc(bv_r, 1)
                if t == T_PR + 6:
                    dve.wait_ge(sg_t, NG * h + 1)
                    dve.scalar_tensor_tensor(out=sg[:, 0, :], in0=sg[:, 0, :], scalar=1.0, in1=A[1][:, :],
                                             op0=ALU.add, op1=ALU.mult).then_inc(sg_r, 1)
                if t == T_PR + 7:
                    dve.wait_ge(sg_t, NG * h + 2)
                    dve.scalar_tensor_tensor(out=sg[:, 1, :], in0=sg[:, 1, :], scalar=1.0, in1=A[0][:, :],
                                             op0=ALU.add, op1=ALU.mult).then_inc(sg_r, 1)
                    if h == 0:
                        dve.memset(S[:, :, 0:1], 0.0).then_inc(s_zero, 1)
                if T_SC <= t < T_SC + NV // 2:
                    scan(h, 2 * (t - T_SC))
                    scan(h, 2 * (t - T_SC) + 1)
                if t == T_SC + 10:
                    take_o(h, 0)
                if t == T_SC + 18:
                    take_o(h, 1)
                if t == T_PO + 5:
                    group_norm(h)
                if t == T_PO + 6:
                    for b in range(NB):
                        dve.wait_ge(yp, NB * h + b + 1)
                        dve.tensor_tensor(xT[:, h, b, :], A[2 * (1 - b)][:, :], xT[:, h, b, :], ALU.add).then_inc(x_att, 1)

            def route_a2(s):
                route_b(s, 0)
                route_a(s, 1)

            dve.memset(epsc[:, :], EPS).then_inc(setup, 1)
            for b in range(NB):
                stats(b, 1 - b)
            for b in range(NB):
                normalise(b, 1 - b)
            dve.wait_ge(small_l, 16)
            link(dve.tensor_copy(rwh[:, 0, :], w(W_RT, E)))
            dve.tensor_tensor(rwh[:, 1, :], w(W_RT, E), rwh[:, 0, :], ALU.subtract).then_inc(rw_r, 1)
            ffn_lo(0, 0)
            split_w(0)
            ffn_lo(0, 1)
            for b in range(NB):
                route_a(0, b)
                route_b(0, b)
            split_w(1)
            for s, (half, h) in enumerate(STAGES):
                for i in range(STEPS):
                    g = s * STEPS + i
                    for f in range(FC):
                        split_h(g * FC + f)
                        if g > 0 and f == FC - 1:
                            combine(g - 1)
                        beside(s, h, 4 * i + f)
                    if s == 0 and i + 2 < E:
                        split_w(i + 2)
                if s == 0:
                    ffn_lo(1, 1)
                if h is not None:
                    for b in range(NB):
                        stats(LN_FFN[s + 1] + b, 1 - b)
                    for b in range(NB):
                        normalise(LN_FFN[s + 1] + b, 1 - b)
                    for b in range(NB):
                        ffn_lo(s + 1, b)
            combine(4 * STEPS - 1)

        @block.gpsimd
        def _(pool):
            def add_y(g):
                s, i = divmod(g, STEPS)
                pool.wait_ge(comb, g + 1)
                if g >= 1:
                    pool.wait_ge(acc, g)
                dst = xT[:, STAGES[s][0], i // E, :]
                pool.tensor_tensor(dst, dst, gy[:, g % 2, :], ALU.add).then_inc(acc, 1)

            def read_state(h, m):
                n = h * NV + m
                pool.wait_ge(st_r, n + 1)
                if n >= QS:
                    pool.wait_ge(red, (n - QS) // 4 + 1)
                if h == 0:
                    pool.tensor_copy(carry[:, m:m + 1], S[:, n % SS, NT:NT + 1]).then_inc(pch, 1)
                else:
                    pool.wait_ge(seed, m + 1)
                pool.tensor_tensor(qs[:, n % QS, :], q[:, :], S[:, n % SS, 0:NT], ALU.mult).then_inc(qs_r, 1)

            def seed_state(m):
                n = NV + m
                pool.wait_ge(pch, m + 1)
                pool.wait_ge(qs_r, n - SS + 1)
                pool.tensor_copy(S[:, n % SS, 0:1], carry[:, m:m + 1]).then_inc(seed, 1)

            def beside(s, h, t):
                if h is None:
                    return
                if T_MUS <= t < T_MUS + 10:
                    n = t - T_MUS
                    i, b = MIX[n // NB], n % NB
                    pool.wait_ge(mterm, 10 * h + n + 1)
                    pool.tensor_tensor(u[:, i, b, :], u[:, i, b, :], xa[:, b, 1:NT + 1], ALU.add).then_inc(u_r, 1)
                    if h == 0 and n == 9:
                        pool.wait_ge(u_r, 10)
                        pool.tensor_copy(xa[:, :, 0:1], xa[:, :, NT:NT + 1]).then_inc(xa_prev, 1)
                if t == T_SC:
                    if h == 0:
                        pool.wait_ge(s_zero, 1)
                    else:
                        pool.wait_ge(pr, 14)
                        for m in range(2):
                            seed_state(m)
                if T_SC <= t < T_SC + NV // 2:
                    for m in (2 * (t - T_SC), 2 * (t - T_SC) + 1):
                        read_state(h, m)
                        if h == 1 and m + 2 < NV:
                            seed_state(m + 2)

            for s, (half, h) in enumerate(STAGES):
                for i in range(STEPS):
                    g = s * STEPS + i
                    for f in range(FC):
                        if g > 0 and f == FC - 1:
                            add_y(g - 1)
                        beside(s, h, 4 * i + f)
            add_y(4 * STEPS - 1)


def order(m):
    g, r = divmod(m, VG)
    n, c = divmod(r, 4)
    return g, 4 * c + n


def lay_out(d):
    import numpy as np
    f = np.float32
    x = np.asarray(d["L0_attn_hidden_states"])
    xT = np.ascontiguousarray(x.reshape(NB, 2, NT, P).transpose(3, 1, 0, 2).reshape(P, 2 * NB * NT))
    w1, w2 = np.asarray(d["L0_ffn_w1"]), np.asarray(d["L0_ffn_w2"])
    wexp = np.zeros((P, E, 2, FC, P), f)
    wexp[:, :, 0] = w1.reshape(E, FC, P, P).transpose(3, 0, 1, 2)
    wexp[:, :, 1] = w2.reshape(E, P, FC, P).transpose(3, 0, 2, 1)
    s = np.zeros((P, W_ALL), f)
    g = {k[8:]: np.asarray(v) for k, v in d.items() if k.startswith("L0_attn_")}
    s[:, W_X1:W_X1 + 160] = g["W_x1"].T
    x2 = g["W_x2"].reshape(P, 5, 32).transpose(1, 2, 0)
    s[:, W_X2:W_X2 + P] = x2[:4].reshape(P, P)
    s[0:32, W_X2B:W_X2B + P] = s[32:64, W_X2B:W_X2B + P] = x2[4]
    s[:, W_R:W_R + 64] = g["W_r"].T
    s[:, W_K:W_K + 64] = g["W_k"].T
    s[:, W_A:W_A + 64] = g["A_w"].T
    s[0:64, W_B:W_B + 64] = s[64:128, W_B:W_B + 64] = g["B_w"].T
    for at, name in ((W_V, "W_v"), (W_G, "W_g")):
        v = s[:, at:at + NG * NB * P].reshape(P, NG, NB, VG, NB, NH)
        src = g[name].reshape(NH, NG, VG, P).transpose(3, 1, 2, 0)
        for b in range(NB):
            v[:, :, b, :, b, :] = src
        s[:, at:at + NG * NB * P] = v.reshape(P, -1)
    v = np.zeros((VG, NB, NH, NG, NB, P), f)
    src = g["W_o"].reshape(P, NH, NG, VG).transpose(3, 1, 2, 0)
    for b in range(NB):
        v[:, b, :, :, b, :] = src
    s[:, W_O:W_O + NG * NB * P] = v.reshape(P, -1)
    s[:, W_RT:W_RT + E] = np.asarray(d["L0_ffn_router_w"]).T
    s[:, W_B1:W_B1 + E * FC] = np.asarray(d["L0_ffn_b1"]).reshape(E * FC, P).T
    s[:, W_B2:W_B2 + E] = np.asarray(d["L0_ffn_b2"]).T
    s[:, W_MU] = g["mu_x"]
    s[:, W_XB:W_XB + 5] = g["x_bias"].T
    s[:, W_BW] = np.tile(g["b_w"], NB)
    s[:, W_U] = np.tile(g["bonus"].reshape(-1), NB)
    for at, name in ((W_GW, "gn_weight"), (W_GB, "gn_bias")):
        src = g[name].reshape(NH, NG, VG).transpose(2, 0, 1)
        s[:, at:at + NG] = np.broadcast_to(src[:, None], (VG, NB, NH, NG)).reshape(P, NG)
    c = np.zeros((P, C_ALL), f)
    eye = np.eye(P, dtype=f)
    c[:, C_ID:C_ID + P] = eye
    bh_v, v_of = np.arange(P) % BH, np.arange(P) // BH
    bh_k = np.arange(P) // KD
    for j in range(VG):
        c[:, C_SEL + j * P:C_SEL + (j + 1) * P] = (v_of[:, None] == j) & (bh_v[:, None] == bh_k[None, :])
    for n in range(4):
        cols = np.arange(32)
        c[:, C_RED + 32 * n:C_RED + 32 * n + 32] = (cols[None, :] // BH == n) & (cols[None, :] % BH == bh_k[:, None])
    same = (bh_v[:, None] == bh_v[None, :]).astype(f) / NV
    c[:, C_CEN:C_CEN + P] = eye - same
    c[:, C_CEN + P:C_CEN + 2 * P] = -same
    c[:, C_AVG:C_AVG + P] = same
    c[:, C_BET:C_BET + P] = bh_k[:, None] == bh_v[None, :]
    c[:, C_TIE:C_TIE + 64] = np.tile(E - np.arange(E), 8)[None, :]
    return {"xT_dram": xT, "wexp_dram": wexp.reshape(P, -1), "small_dram": s, "const_dram": c}


def kernel(**inputs):
    import numpy as np
    import concourse.bacc as bacc
    from concourse.bass_utils import run_bass_kernel_spmd as run

    arrays = lay_out(inputs)
    nc = bacc.Bacc("TRN2", target_bir_lowering=False, num_devices=1)
    args = [nc.dram_tensor(n, a.shape, F32, kind="ExternalInput").ap() for n, a in arrays.items()]
    out = nc.dram_tensor("out_dram", (P, 2 * NB * NT), F32, kind="ExternalOutput").ap()
    program(nc, *args, out)
    r = run(nc, [arrays], core_ids=[0])
    y = r.results[0]["out_dram"].reshape(P, 2, NB, NT)
    return np.ascontiguousarray(y.transpose(2, 1, 3, 0).reshape(NB, 2 * NT, P))
```
